# Optimizing a Trainium2 kernel written in Bass

```python
import numpy as np
import jax
import jax.numpy as jnp

def _softmax(x, axis=-1):
    return jax.nn.softmax(x, axis=axis)

def _gelu(x):
    return jax.nn.gelu(x, approximate=True)

def _silu(x):
    return jax.nn.silu(x)

def _sigmoid(x):
    return jax.nn.sigmoid(x)

def _layernorm(x, axis=-1, eps=1e-05):
    m = jnp.mean(x, axis=axis, keepdims=True)
    v = jnp.var(x, axis=axis, keepdims=True)
    return (x - m) / jnp.sqrt(v + eps)

def _scatter_add(tgt, idx, src, axis=0):
    return tgt.at[idx].add(src)

def _segment_sum(src, seg, n):
    return jax.ops.segment_sum(src, seg, n)
kernel_name = 'mk_prb_d1_jaxref_r8_5e906a'

def setup_inputs(seed: int=0):
    np.random.seed(seed)
    _w = jnp.asarray

    def _L0_attn_setup():
        import jax, jax.numpy as jnp
        import numpy as np
        EMB = 512
        HEADS = 32
        SCALE = 4
        D = EMB // HEADS
        HKV = HEADS // SCALE
        B, S = (2, 256)
        key = jax.random.key(seed)
        ks = jax.random.split(key, 7)
        std = 0.02
        return {'x': jax.random.normal(ks[0], (B, S, EMB), jnp.float32), 'Wq': jax.random.normal(ks[1], (EMB, D, HEADS), jnp.float32) * std, 'bq': jnp.zeros((D, HEADS), jnp.float32), 'Wk': jax.random.normal(ks[2], (EMB, D, HKV), jnp.float32) * std, 'bk': jnp.zeros((D, HKV), jnp.float32), 'Wv': jax.random.normal(ks[3], (EMB, D, HKV), jnp.float32) * std, 'bv': jnp.zeros((D, HKV), jnp.float32)}
    _L0_attn_in = _L0_attn_setup()

    def _L0_ffn_setup():
        import jax, jax.numpy as jnp
        import numpy as np
        BS = 128
        FP8_MAX = 448.0

        def act_quant(x):
            T, K = x.shape
            xb = x.reshape(T, K // BS, BS)
            amax = jnp.max(jnp.abs(xb), axis=-1)
            scale = amax / FP8_MAX + 1e-12
            xq = (xb / scale[:, :, None]).reshape(T, K)
            return (xq, scale)

        def linear_dsv3(x, wq, w_scale):
            T, K = x.shape
            N = wq.shape[0]
            xq, xs = act_quant(x)
            xdq = (xq.reshape(T, K // BS, BS) * xs[:, :, None]).reshape(T, K)
            wdq = (wq.reshape(N // BS, BS, K // BS, BS) * w_scale[:, None, :, None]).reshape(N, K)
            return xdq @ wdq.T
        key = jax.random.key(seed)
        ks = jax.random.split(key, 4)
        DIM, INTER = (512, 1792)

        def make_qweight(k, n, m):
            w = jax.random.normal(k, (n, m), dtype=jnp.float32) * 0.02
            wb = w.reshape(n // BS, BS, m // BS, BS)
            amax = jnp.max(jnp.abs(wb), axis=(1, 3))
            scale = amax / FP8_MAX + 1e-12
            wq = (wb / scale[:, None, :, None]).reshape(n, m)
            return (wq, scale)
        x = jax.random.normal(ks[0], (2, 128, DIM), dtype=jnp.float32)
        w1, w1_scale = make_qweight(ks[1], INTER, DIM)
        w3, w3_scale = make_qweight(ks[2], INTER, DIM)
        w2, w2_scale = make_qweight(ks[3], DIM, INTER)
        return {'x': x, 'w1': w1, 'w1_scale': w1_scale, 'w3': w3, 'w3_scale': w3_scale, 'w2': w2, 'w2_scale': w2_scale}
    _L0_ffn_in = _L0_ffn_setup()
    _d = {'L0_attn_x': _L0_attn_in['x'], 'L0_attn_Wq': _L0_attn_in['Wq'], 'L0_attn_bq': _L0_attn_in['bq'], 'L0_attn_Wk': _L0_attn_in['Wk'], 'L0_attn_bk': _L0_attn_in['bk'], 'L0_attn_Wv': _L0_attn_in['Wv'], 'L0_attn_bv': _L0_attn_in['bv'], 'L0_ffn_w1': _L0_ffn_in['w1'], 'L0_ffn_w1_scale': _L0_ffn_in['w1_scale'], 'L0_ffn_w3': _L0_ffn_in['w3'], 'L0_ffn_w3_scale': _L0_ffn_in['w3_scale'], 'L0_ffn_w2': _L0_ffn_in['w2'], 'L0_ffn_w2_scale': _L0_ffn_in['w2_scale']}
    _x0 = _d['L0_attn_x']
    _d['L0_attn_x'] = jax.random.normal(jax.random.fold_in(jax.random.key(seed), 1), (2, 1024, 512), dtype=_x0.dtype)
    del _x0
    return _d

def reference(L0_attn_x, L0_attn_Wq, L0_attn_bq, L0_attn_Wk, L0_attn_bk, L0_attn_Wv, L0_attn_bv, L0_ffn_w1, L0_ffn_w1_scale, L0_ffn_w3, L0_ffn_w3_scale, L0_ffn_w2, L0_ffn_w2_scale):

    def _L0_attn_ref(x, Wq, bq, Wk, bk, Wv, bv):
        import jax, jax.numpy as jnp
        import numpy as np
        EMB = 512
        HEADS = 32
        SCALE = 4
        D = EMB // HEADS
        HKV = HEADS // SCALE
        B, S = (2, 256)
        q = jnp.einsum('bse,edh->bsdh', x, Wq) + bq
        k = jnp.einsum('bse,edh->bsdh', x, Wk) + bk
        v = jnp.einsum('bse,edh->bsdh', x, Wv) + bv
        k = jnp.repeat(k, SCALE, axis=-1)
        v = jnp.repeat(v, SCALE, axis=-1)
        scores = jnp.einsum('bsdh,bseh->bsde', q, k) / np.float32(np.sqrt(D))
        attn = jax.nn.softmax(scores, axis=-1)
        out = jnp.einsum('bsde,bseh->bsdh', attn, v)
        return out.reshape(x.shape[:-1] + (EMB,))

    def _L0_ffn_ref(x, w1, w1_scale, w3, w3_scale, w2, w2_scale):
        import jax, jax.numpy as jnp
        import numpy as np
        BS = 128
        FP8_MAX = 448.0

        def act_quant(x):
            T, K = x.shape
            xb = x.reshape(T, K // BS, BS)
            amax = jnp.max(jnp.abs(xb), axis=-1)
            scale = amax / FP8_MAX + 1e-12
            xq = (xb / scale[:, :, None]).reshape(T, K)
            return (xq, scale)

        def linear_dsv3(x, wq, w_scale):
            T, K = x.shape
            N = wq.shape[0]
            xq, xs = act_quant(x)
            xdq = (xq.reshape(T, K // BS, BS) * xs[:, :, None]).reshape(T, K)
            wdq = (wq.reshape(N // BS, BS, K // BS, BS) * w_scale[:, None, :, None]).reshape(N, K)
            return xdq @ wdq.T
        B, S, D = x.shape
        xf = x.reshape(-1, D)
        g = linear_dsv3(xf, w1, w1_scale)
        u = linear_dsv3(xf, w3, w3_scale)
        h = jax.nn.silu(g) * u
        y = linear_dsv3(h, w2, w2_scale)
        return y.reshape(B, S, D)
    x = L0_attn_x
    xn = _layernorm(x, axis=-1)
    x = x + _L0_attn_ref(xn, L0_attn_Wq, L0_attn_bq, L0_attn_Wk, L0_attn_bk, L0_attn_Wv, L0_attn_bv) + _L0_ffn_ref(xn, L0_ffn_w1, L0_ffn_w1_scale, L0_ffn_w3, L0_ffn_w3_scale, L0_ffn_w2, L0_ffn_w2_scale)
    return x

_drawn_inputs = setup_inputs


def setup_inputs(seed=0):
    import zlib

    import numpy as np

    out = dict(_drawn_inputs(seed))
    spreads = {'L0_attn_bq': (0.0, 2.0), 'L0_attn_bk': (0.0, 2.0), 'L0_attn_bv': (0.0, 2.0)}
    factors = {'L0_ffn_w1_scale': 6.997,
     'L0_ffn_w3_scale': 6.788,
     'L0_ffn_w2_scale': 8.0,
     'L0_attn_Wq': 8.0,
     'L0_attn_Wk': 8.0,
     'L0_attn_Wv': 8.0}
    for name, (base, spread) in spreads.items():
        noise = np.random.default_rng([zlib.crc32(name.encode()), seed]).standard_normal(out[name].shape)
        drawn = base * np.exp(spread * noise) if base else spread * noise
        out[name] = jnp.asarray(drawn.astype(out[name].dtype))
    for name, factor in factors.items():
        out[name] = (out[name] * factor).astype(out[name].dtype)
    return out
```

```python
from contextlib import ExitStack

import concourse.bass as bass
from concourse import mybir

F32 = mybir.dt.float32
F32R = mybir.dt.float32r
I32 = mybir.dt.int32
ALU = mybir.AluOpType
ACT = mybir.ActivationFunctionType
AX = mybir.AxisListType

P = 128
EPS = 1e-5
RSQRT_MAGIC = 0x5F3759DF
NEWTON = 3


def fused_block(nc, x, wq, bq, wk, bk, wv, bv, w_all, scales, identity, out):
    B, S, E = x.shape
    T = B * S
    D, HKV = wk.shape[1], wk.shape[2]
    H = wq.shape[2]
    REP = H // HKV
    KB = E // P
    NBLK, _, MATS, _ = w_all.shape
    TILES = T // P
    CHUNK = 512
    TPC = CHUNK // P
    CHUNKS = T // CHUNK
    GB = 2
    GROUPS = NBLK // GB
    QKV = 3 * D * HKV
    DH = D * HKV
    RING = 2 * GB
    GATE, UP, DOWN = 0, 1, 2

    LOOPS = (GROUPS - 1) // 2
    STEPS = 2 * CHUNKS
    ATT = (TILES - 1) // LOOPS
    ATT_OPS = 10
    assert CHUNKS == TPC == KB == 4 and T == 2048 and E == 512 and D * REP * HKV == E and DH == P
    assert 1 + ATT * LOOPS == TILES and 1 + 2 * LOOPS == GROUPS and 3 * ATT <= 2 * STEPS

    x_tiles = x.rearrange("b s e -> (b s) e").rearrange("(t p) e -> t p e", p=P)
    out_tiles = out.rearrange("b s e -> (b s) e").rearrange("(t p) e -> t p e", p=P)
    qkv_spill = nc.dram_tensor("qkv_spill", [TILES, P, QKV], F32, kind="Internal").ap()

    with ExitStack() as ctx:
        def sb(name, shape, dt=F32):
            return ctx.enter_context(nc.sbuf_tensor(name, shape, dt))

        def sem(name):
            return ctx.enter_context(nc.semaphore(name))

        acc = sb("acc", [P, TILES, E])
        xT_hi = sb("xT_hi", [P, KB, T], F32R)
        xT_lo = sb("xT_lo", [P, KB, T], F32R)
        w_raw = sb("w_raw", [P, 2, MATS, E])
        w_hi = sb("w_hi", [P, RING, MATS, E], F32R)
        w_lo = sb("w_lo", [P, RING, MATS, E], F32R)
        h_hi = sb("h_hi", [P, 2, GB, CHUNK], F32R)
        h_lo = sb("h_lo", [P, 2, GB, CHUNK], F32R)
        hidden = sb("hidden", [P, GB, CHUNK])
        wqkv_hi = sb("wqkv_hi", [P, KB, QKV], F32R)
        wqkv_lo = sb("wqkv_lo", [P, KB, QKV], F32R)
        scratch = sb("scratch", [P, TPC, E])
        qkv = sb("qkv", [P, 3, QKV])
        bias = sb("bias", [P, QKV])
        scale = sb("scale", [P, NBLK, MATS * KB])
        ident = sb("ident", [P, P])
        scores = sb("scores", [P, D, D])
        top = sb("top", [P, D])
        total = sb("total", [P, D])
        att_out = sb("att_out", [P, DH])
        stats = sb("stats", [P, TPC, 6])
        mean_var = sb("mean_var", [P, TPC, 2])
        var = sb("var", [P, TPC])
        rstd = sb("rstd", [P, TPC])
        newton = sb("newton", [P, TPC])

        BORROWED = 8
        bq_raw = acc[:, 8, :]
        wq_sum = acc[:, 9, :].rearrange("p (kb n) -> p kb n", kb=KB)
        wk_raw = acc[:, 10, :].rearrange("p (kb n) -> p kb n", kb=KB)
        wv_raw = acc[:, 11, :].rearrange("p (kb n) -> p kb n", kb=KB)
        wq_raw = acc[:, 12:16, :]

        ps_gu = ctx.enter_context(nc.psum_tensor("ps_gu", [P, GB, 2, CHUNK], F32))
        ps_y = ctx.enter_context(nc.psum_tensor("ps_y", [P, 4, E], F32))
        ps_t = ps_y[:, 2, :]
        ps_qkv = ps_y[:, 3, 0:QKV]

        x_in = [sem(f"x_in{t}") for t in range(TILES)]
        ident_in, scale_in, bias_in, wqkv_in = sem("ident_in"), sem("scale_in"), sem("bias_in"), sem("wqkv_in")
        w_in = [sem(f"w_in{i}") for i in range(2)]
        qkv_out = [sem(f"qkv_out{i}") for i in range(2)]
        qkv_in = [sem(f"qkv_in{i}") for i in range(3)]
        stored = sem("stored")
        ln_ops, xn_done, t_done = sem("ln_ops"), sem("xn_done"), sem("t_done")
        xhi_done, xlo_done = sem("xhi_done"), sem("xlo_done")
        w_dequant, whi_done, wlo_done = sem("w_dequant"), sem("whi_done"), sem("wlo_done")
        qsum_done, qkvw_hi, qkvw_lo = sem("qsum_done"), sem("qkvw_hi"), sem("qkvw_lo")
        qkv_done, qkv_evac = sem("qkv_done"), sem("qkv_evac")
        g_done, u_done, silu_done, prod_done = sem("g_done"), sem("u_done"), sem("silu_done"), sem("prod_done")
        hhi_done, hlo_done = sem("hhi_done"), sem("hlo_done")
        y_done, y_added = sem("y_done"), sem("y_added")
        att_ops, exp_done = sem("att_ops"), sem("exp_done")

        block = ctx.enter_context(nc.Block())

        def steps(i, s):
            return i * STEPS + s

        def wait(eng, sem_, i, rate, n):
            if isinstance(i, int):
                if n + rate * i > 0:
                    eng.wait_ge(sem_, n + rate * i)
            else:
                eng.wait_ge(sem_, i * rate + n)

        def next_block(s):
            c = s % CHUNKS
            return GB * (s // CHUNKS + 1) + c - 1 if c in (1, 2) else None

        W_RATE = MATS * 2 * GB

        def block_index(i, n):
            if isinstance(i, int):
                return n
            return nc.s_assert_within(i * 2 * GB + n, n, NBLK - 1,
                                      skip_runtime_bounds_check_because="guarded by If in the last turn")

        def att_piece(q):
            return divmod(q, 3) if q < 3 * ATT else None

        def past_last_block(s):
            return s >= 2 * CHUNKS

        @block.sync
        def _(sp):
            def load_w(i, n):
                if not isinstance(i, int) or n >= 2:
                    wait(sp, wlo_done, i, W_RATE, MATS * (n - 1))
                sp.dma_start(w_raw[:, n % 2], w_all[block_index(i, n)]).then_inc(w_in[n % 2], 16)

            def load_qkv(i, t, slot):
                sp.dma_start(qkv[:, slot], qkv_spill[i * ATT + t]).then_inc(qkv_in[slot], 16)

            for t in range(TPC):
                sp.dma_start(acc[:, t], x_tiles[t]).then_inc(x_in[t], 16)
                if t == 0:
                    sp.dma_start(ident[:], identity).then_inc(ident_in, 16)
                    sp.dma_start(scale[:], scales.rearrange("(o n) m -> o n m", o=1)
                                 .broadcast_to([P, NBLK, MATS * KB])).then_inc(scale_in, 16)
            load_w(0, 0)
            load_w(0, 1)
            for t in range(TPC, BORROWED):
                sp.dma_start(acc[:, t], x_tiles[t]).then_inc(x_in[t], 16)
            sp.dma_start(wq_raw, wq.rearrange("(kb p) d h -> p kb (d h)", p=P)).then_inc(wqkv_in, 16)
            sp.dma_start(wk_raw, wk.rearrange("(kb p) d h -> p kb (d h)", p=P)).then_inc(wqkv_in, 16)
            sp.dma_start(wv_raw, wv.rearrange("(kb p) d h -> p kb (d h)", p=P)).then_inc(wqkv_in, 16)
            sp.dma_start(bq_raw, bq.rearrange("(o d) h -> o (d h)", o=1).broadcast_to([P, D * H])).then_inc(bias_in, 16)
            sp.dma_start(bias[:, DH:2 * DH], bk.rearrange("(o d) h -> o (d h)", o=1).broadcast_to([P, DH])).then_inc(bias_in, 16)
            sp.dma_start(bias[:, 2 * DH:], bv.rearrange("(o d) h -> o (d h)", o=1).broadcast_to([P, DH])).then_inc(bias_in, 16)
            sp.wait_ge(qkvw_lo, 3)
            sp.wait_ge(qsum_done, 2)
            for t in range(BORROWED, TILES):
                sp.dma_start(acc[:, t], x_tiles[t]).then_inc(x_in[t], 16)
            for c in range(CHUNKS):
                for t in range(TPC * c, TPC * c + TPC):
                    sp.wait_ge(qkv_evac, t + 1)
                    sp.dma_start(qkv_spill[t], qkv[:, t % 2]).then_inc(qkv_out[t % 2], 16)
                if c == 0:
                    load_w(0, 2)
                    load_w(0, 3)
                if c == CHUNKS - 2:
                    sp.wait_ge(qkv_out[0], 16)
                    load_qkv(0, 0, 2)
            for slot in range(2):
                sp.wait_ge(qkv_out[slot], 16 * TILES // 2)
            with sp.Fori(0, LOOPS) as i:
                for s in range(CHUNKS, CHUNKS + STEPS):
                    for q in (2 * (s - CHUNKS), 2 * (s - CHUNKS) + 1):
                        piece = att_piece(q)
                        if piece and piece[1] == 0:
                            j = piece[0]
                            wait(sp, att_ops, i, ATT_OPS * ATT, ATT_OPS * (j if j == 0 else j - 1) + 7)
                            load_qkv(i, 1 + j, j % 2)
                    if s % CHUNKS == 0:
                        n = GB * (s // CHUNKS + 1)
                        if past_last_block(s):
                            with sp.If(i < LOOPS - 1):
                                load_w(i, n)
                                load_w(i, n + 1)
                        else:
                            load_w(i, n)
                            load_w(i, n + 1)
            for t in range(TILES):
                sp.wait_ge(y_added, TILES * (GROUPS - 1) + t + 1)
                sp.dma_start(out_tiles[t], acc[:, t]).then_inc(stored, 16)
            sp.wait_ge(stored, 16 * TILES)

        @block.tensor
        def _(pe):
            def transpose_tile(t):
                pe.wait_ge(xn_done, t + 1)
                if t >= 1:
                    pe.wait_ge(xlo_done, t)
                for kb in range(KB):
                    last = pe.transpose(ps_t[:, kb * P:(kb + 1) * P], scratch[:, t % TPC, kb * P:(kb + 1) * P], ident[:])
                last.then_inc(t_done, 1)

            def qkv_tile(t):
                if t == 0:
                    pe.wait_ge(qkvw_lo, 3)
                if t >= 1:
                    pe.wait_ge(qkv_evac, t)
                cols = slice(t * P, (t + 1) * P)
                parts = ((xT_hi, wqkv_hi), (xT_hi, wqkv_lo), (xT_lo, wqkv_hi))
                for n, (xt, w) in enumerate(parts):
                    for kb in range(KB):
                        last = pe.matmul(ps_qkv, xt[:, kb, cols], w[:, kb, :],
                                         start=(n == 0 and kb == 0), stop=(n == 2 and kb == KB - 1))
                last.then_inc(qkv_done, 1)

            def gate_up(i, s, b):
                c, g, k = s % CHUNKS, s // CHUNKS, GB * s + b
                n = GB * g + b
                cols = slice(c * CHUNK, (c + 1) * CHUNK)
                for m, done, freed in ((GATE, g_done, silu_done), (UP, u_done, prod_done)):
                    if c == 0:
                        wait(pe, whi_done, i, W_RATE, MATS * n + m + 1)
                    wait(pe, freed, i, GB * STEPS, k - 1)
                    for n3, (w, xt) in enumerate(((w_hi, xT_hi), (w_hi, xT_lo), (w_lo, xT_hi))):
                        if c == 0 and n3 == 2:
                            wait(pe, wlo_done, i, W_RATE, MATS * n + m + 1)
                        for kb in range(KB):
                            last = pe.matmul(ps_gu[:, b, m, :], w[:, n % RING, m, kb * P:(kb + 1) * P], xt[:, kb, cols],
                                             start=(n3 == 0 and kb == 0), stop=(n3 == 2 and kb == KB - 1))
                    last.then_inc(done, 1)

            def down(i, s, banks):
                c, g = s % CHUNKS, s // CHUNKS
                if c == 0:
                    wait(pe, wlo_done, i, W_RATE, MATS * GB * (g + 1))
                wait(pe, hlo_done, i, GB * STEPS, GB * (s + 1))
                if banks == 4:
                    wait(pe, y_added, i, TPC * STEPS, TPC * s)
                for tt in range(TPC):
                    if banks == 2:
                        wait(pe, y_added, i, 0, TPC * s + tt - 1)
                    rows = slice(tt * P, (tt + 1) * P)
                    for b in range(GB):
                        r = (GB * g + b) % RING
                        for n3, (h, w) in enumerate(((h_hi, w_hi), (h_hi, w_lo), (h_lo, w_hi))):
                            last = pe.matmul(ps_y[:, tt % banks, :], h[:, s % 2, b, rows], w[:, r, DOWN, :],
                                             start=(b == 0 and n3 == 0), stop=(b == GB - 1 and n3 == 2))
                    last.then_inc(y_done, 1)

            pe.wait_ge(ident_in, 16)
            for t in range(TPC):
                transpose_tile(t)
            for s in range(CHUNKS):
                pe.wait_ge(xlo_done, TPC * (s + 1))
                for b in range(GB):
                    gate_up(0, s, b)
                if s >= 1:
                    down(0, s - 1, 2)
                for j in range(TPC):
                    if s + 1 < CHUNKS:
                        transpose_tile(TPC * (s + 1) + j)
                    qkv_tile(TPC * s + j)
            pe.wait_ge(qkv_evac, TILES)
            with pe.Fori(0, LOOPS) as i:
                for s in range(CHUNKS, CHUNKS + STEPS):
                    for b in range(GB):
                        gate_up(i, s, b)
                    down(i, s - 1, 4)
            down(LOOPS, CHUNKS - 1, 4)

        @block.scalar
        def _(act):
            def split_hi(i, n, m):
                wait(act, w_dequant, i, W_RATE, MATS * n + m + 1)
                if m == 0 and n >= RING:
                    wait(act, y_done, i, TPC * STEPS, TPC * CHUNKS * (n // GB - 1))
                nc.scalar.copy(w_hi[:, n % RING, m], w_raw[:, n % 2, m]).then_inc(whi_done, 1)

            def silu(i, s, b):
                k = GB * s + b
                wait(act, g_done, i, GB * STEPS, k + 1)
                wait(act, hlo_done, i, GB * STEPS, k - 1)
                nc.scalar.activation(hidden[:, b], ps_gu[:, b, GATE, :], ACT.Silu).then_inc(silu_done, 1)

            def hidden_hi(i, s, b):
                k = GB * s + b
                wait(act, prod_done, i, GB * STEPS, k + 1)
                wait(act, y_done, i, TPC * STEPS, TPC * (s - 1))
                nc.scalar.copy(h_hi[:, s % 2, b], hidden[:, b]).then_inc(hhi_done, 1)

            def x_hi(t):
                act.wait_ge(t_done, t + 1)
                nc.scalar.copy(xT_hi[:, :, t * P:(t + 1) * P],
                               ps_t.rearrange("p (kb n) -> p kb n", kb=KB)).then_inc(xhi_done, 1)

            def exponent(i, t):
                wait(act, att_ops, i, ATT_OPS * ATT, ATT_OPS * t + 4)
                nc.scalar.activation(scores[:], scores[:], ACT.Exp, scale=float(D) ** -0.5).then_inc(exp_done, 1)

            def prepare(i, s):
                n = next_block(s)
                if n is not None:
                    for m in range(MATS):
                        split_hi(i, n, m)

            x_hi(0)
            x_hi(1)
            split_hi(0, 0, 0)
            x_hi(2)
            x_hi(3)
            for n, m in ((0, 1), (0, 2), (1, 0), (1, 1), (1, 2)):
                split_hi(0, n, m)
            act.wait_ge(wqkv_in, 48)
            act.wait_ge(qsum_done, 1)
            for n, raw in enumerate((wq_sum, wk_raw, wv_raw)):
                nc.scalar.copy(wqkv_hi[:, :, n * DH:(n + 1) * DH], raw).then_inc(qkvw_hi, 1)
            for s in range(CHUNKS):
                for b in range(GB):
                    silu(0, s, b)
                    if s == CHUNKS - 1 and b == 0:
                        exponent(0, 0)
                    hidden_hi(0, s, b)
                prepare(0, s)
                if s + 1 < CHUNKS:
                    for j in range(TPC):
                        x_hi(TPC * (s + 1) + j)
            with act.Fori(0, LOOPS) as i:
                for s in range(CHUNKS, CHUNKS + STEPS):
                    for b in range(GB):
                        silu(i, s, b)
                        piece = att_piece(2 * (s - CHUNKS) + b)
                        if piece and piece[1] == 0:
                            exponent(i, 1 + piece[0])
                        hidden_hi(i, s, b)
                    if past_last_block(s) and next_block(s) is not None:
                        with act.If(i < LOOPS - 1):
                            prepare(i, s)
                    else:
                        prepare(i, s)

        @block.gpsimd
        def _(pool):
            def split_lo(i, n, m):
                wait(pool, whi_done, i, W_RATE, MATS * n + m + 1)
                nc.gpsimd.tensor_tensor(w_lo[:, n % RING, m], w_raw[:, n % 2, m], w_hi[:, n % RING, m].bitcast(F32),
                                        ALU.subtract).then_inc(wlo_done, 1)

            def hidden_lo(i, s, b):
                wait(pool, hhi_done, i, GB * STEPS, GB * s + b + 1)
                nc.gpsimd.tensor_tensor(h_lo[:, s % 2, b], hidden[:, b], h_hi[:, s % 2, b].bitcast(F32),
                                        ALU.subtract).then_inc(hlo_done, 1)

            def prepare(i, s):
                n = next_block(s)
                if n is not None:
                    for m in range(MATS):
                        split_lo(i, n, m)

            for n in range(2):
                for m in range(MATS):
                    split_lo(0, n, m)
            for n, raw in enumerate((wq_sum, wk_raw, wv_raw)):
                pool.wait_ge(qkvw_hi, n + 1)
                nc.gpsimd.tensor_tensor(wqkv_lo[:, :, n * DH:(n + 1) * DH], raw,
                                        wqkv_hi[:, :, n * DH:(n + 1) * DH].bitcast(F32),
                                        ALU.subtract).then_inc(qkvw_lo, 1)
            for s in range(CHUNKS):
                for b in range(GB):
                    hidden_lo(0, s, b)
                prepare(0, s)
            with pool.Fori(0, LOOPS) as i:
                for s in range(CHUNKS, CHUNKS + STEPS):
                    for b in range(GB):
                        hidden_lo(i, s, b)
                    if past_last_block(s) and next_block(s) is not None:
                        with pool.If(i < LOOPS - 1):
                            prepare(i, s)
                    else:
                        prepare(i, s)

        @block.vector
        def _(dve):
            ln = [0]

            def ln_op(ins):
                ln[0] += 1
                ins.then_inc(ln_ops, 1)

            def layernorm(c):
                for j in range(TPC):
                    dve.wait_ge(x_in[TPC * c + j], 16)
                    ln_op(nc.vector.bn_stats(stats[:, j], acc[:, TPC * c + j]))
                dve.wait_ge(ln_ops, ln[0])
                if c >= 1:
                    dve.wait_ge(xn_done, TPC * c)
                for j in range(TPC):
                    ln_op(nc.vector.bn_aggr(mean_var[:, j], stats[:, j]))
                dve.wait_ge(ln_ops, ln[0])
                ln_op(nc.vector.tensor_scalar(var[:], mean_var[:, :, 1], EPS, None, ALU.add))
                dve.wait_ge(ln_ops, ln[0])
                ln_op(nc.vector.tensor_scalar(newton[:].bitcast(I32), var[:].bitcast(I32), 1, None,
                                              ALU.logical_shift_right))
                dve.wait_ge(ln_ops, ln[0])
                ln_op(nc.vector.tensor_scalar(rstd[:].bitcast(I32), newton[:].bitcast(I32), -1.0,
                                              float(RSQRT_MAGIC), ALU.mult, ALU.add))
                for _ in range(NEWTON):
                    dve.wait_ge(ln_ops, ln[0])
                    ln_op(nc.vector.tensor_tensor(newton[:], rstd[:], rstd[:], ALU.mult))
                    dve.wait_ge(ln_ops, ln[0])
                    ln_op(nc.vector.scalar_tensor_tensor(out=newton[:], in0=newton[:], scalar=-0.5, in1=var[:],
                                                         op0=ALU.mult, op1=ALU.mult))
                    dve.wait_ge(ln_ops, ln[0])
                    ln_op(nc.vector.scalar_tensor_tensor(out=rstd[:], in0=newton[:], scalar=1.5, in1=rstd[:],
                                                         op0=ALU.add, op1=ALU.mult))
                dve.wait_ge(ln_ops, ln[0])
                if c >= 1:
                    dve.wait_ge(t_done, TPC * c)
                for j in range(TPC):
                    nc.vector.tensor_scalar(scratch[:, j], acc[:, TPC * c + j], mean_var[:, j, 0:1], rstd[:, j:j + 1],
                                            ALU.subtract, ALU.mult).then_inc(xn_done, 1)

            def x_lo(t):
                dve.wait_ge(xhi_done, t + 1)
                cols = slice(t * P, (t + 1) * P)
                nc.vector.tensor_tensor(xT_lo[:, :, cols], ps_t.rearrange("p (kb n) -> p kb n", kb=KB),
                                        xT_hi[:, :, cols].bitcast(F32), ALU.subtract).then_inc(xlo_done, 1)

            def dequant(i, n, m):
                if m == 0:
                    wait(dve, w_in[n % 2], i, 16 * GB, 16 * (n // 2 + 1))
                w = w_raw[:, n % 2, m].rearrange("p (j n) -> p j n", n=P)
                block_scale = scale[:, block_index(i, n), KB * m:KB * (m + 1)].unsqueeze(2).broadcast_to([P, KB, P])
                nc.vector.tensor_tensor(w, w, block_scale, ALU.mult).then_inc(w_dequant, 1)

            def prepare(i, s):
                n = next_block(s)
                if n is not None:
                    for m in range(MATS):
                        dequant(i, n, m)

            def qkv_bias(t):
                dve.wait_ge(qkv_done, t + 1)
                if t >= 2:
                    dve.wait_ge(qkv_out[t % 2], 16 * (t // 2))
                nc.vector.tensor_tensor(qkv[:, t % 2], ps_qkv, bias[:], ALU.add).then_inc(qkv_evac, 1)

            def hidden_product(i, s, b):
                k = GB * s + b
                wait(dve, silu_done, i, GB * STEPS, k + 1)
                wait(dve, u_done, i, GB * STEPS, k + 1)
                nc.vector.tensor_tensor(hidden[:, b], hidden[:, b], ps_gu[:, b, UP, :], ALU.mult).then_inc(prod_done, 1)

            def add_y(i, s, banks, att_count):
                c = s % CHUNKS
                wait(dve, y_added, i, TPC * STEPS, TPC * s)
                wait(dve, att_ops, i, ATT_OPS * ATT, att_count)
                for tt in range(TPC):
                    wait(dve, y_done, i, TPC * STEPS, TPC * s + tt + 1)
                    a = acc[:, TPC * c + tt]
                    nc.vector.tensor_tensor(a, a, ps_y[:, tt % banks, :], ALU.add).then_inc(y_added, 1)

            prod_deh = scratch[:].rearrange("p a b -> p (a b)").rearrange("p (d e h) -> p d e h", d=D, e=D)
            prod_dhe = scratch[:].rearrange("p a b -> p (a b)").rearrange("p (d h e) -> p d h e", d=D, h=HKV)

            def attention(i, t, slot, loads_rate, loads, piece, s):
                base = ATT_OPS * t

                def done(n):
                    wait(dve, att_ops, i, ATT_OPS * ATT, base + n)

                q = qkv[:, slot, 0:DH].rearrange("p (d h) -> p d h", d=D)
                k = qkv[:, slot, DH:2 * DH].rearrange("p (e h) -> p e h", e=D)
                v = qkv[:, slot, 2 * DH:].rearrange("p (e h) -> p h e", e=D)
                if piece == 0:
                    wait(dve, qkv_in[slot], i, loads_rate, loads)
                    done(0)
                    nc.vector.tensor_tensor(prod_deh, q.unsqueeze(2).broadcast_to([P, D, D, HKV]),
                                            k.unsqueeze(1).broadcast_to([P, D, D, HKV]), ALU.mult).then_inc(att_ops, 1)
                    done(1)
                    nc.vector.tensor_reduce(scores[:], prod_deh, AX.X, ALU.add).then_inc(att_ops, 1)
                    done(2)
                    nc.vector.tensor_reduce(top[:], scores[:], AX.X, ALU.max).then_inc(att_ops, 1)
                    done(3)
                    nc.vector.tensor_tensor(scores[:], scores[:], top[:].unsqueeze(2).broadcast_to([P, D, D]),
                                            ALU.subtract).then_inc(att_ops, 1)
                elif piece == 1:
                    wait(dve, exp_done, i, ATT, t + 1)
                    nc.vector.tensor_reduce(total[:], scores[:], AX.X, ALU.add).then_inc(att_ops, 1)
                    nc.vector.tensor_tensor(prod_dhe, scores[:].unsqueeze(2).broadcast_to([P, D, HKV, D]),
                                            v.unsqueeze(1).broadcast_to([P, D, HKV, D]), ALU.mult).then_inc(att_ops, 1)
                    done(5)
                    nc.vector.reciprocal(total[:], total[:]).then_inc(att_ops, 1)
                else:
                    done(6)
                    nc.vector.tensor_reduce(att_out[:].rearrange("p (d h) -> p d h", d=D), prod_dhe, AX.X,
                                            ALU.add).then_inc(att_ops, 1)
                    done(8)
                    o = att_out[:].rearrange("p (d h) -> p d h", d=D)
                    nc.vector.tensor_tensor(o, o, total[:].unsqueeze(2).broadcast_to([P, D, HKV]),
                                            ALU.mult).then_inc(att_ops, 1)
                    done(9)
                    wait(dve, y_added, i, TPC * STEPS, TPC * (s - 1))
                    a = acc[:, i * ATT + t].rearrange("p (n r) -> p n r", r=REP)
                    nc.vector.tensor_tensor(a, a, att_out[:].unsqueeze(2).broadcast_to([P, DH, REP]),
                                            ALU.add).then_inc(att_ops, 1)

            def loop_attention(i, s, slot_in_step):
                piece = att_piece(2 * (s - CHUNKS) + slot_in_step)
                if piece:
                    j = piece[0]
                    rate = (ATT + 1 - j % 2) // 2
                    attention(i, 1 + j, j % 2, 16 * rate, 16 * (j // 2 + 1), piece[1], s)

            def att_issued(s):
                per_piece = (4, 3, 3)
                slots = 2 * (s - CHUNKS + 1)
                return ATT_OPS + sum(per_piece[q % 3] for q in range(min(slots, 3 * ATT)))

            layernorm(0)
            dve.wait_ge(scale_in, 16)
            dequant(0, 0, 0)
            x_lo(0)
            x_lo(1)
            dequant(0, 0, 1)
            x_lo(2)
            x_lo(3)
            for n, m in ((0, 2), (1, 0), (1, 1), (1, 2)):
                dequant(0, n, m)
            dve.wait_ge(wqkv_in, 48)
            nc.vector.tensor_reduce(wq_sum, wq_raw.rearrange("p kb (n r) -> p kb n r", r=REP), AX.X,
                                    ALU.add).then_inc(qsum_done, 1)
            dve.wait_ge(bias_in, 48)
            nc.vector.tensor_reduce(bias[:, 0:DH], bq_raw.rearrange("p (n r) -> p n r", r=REP), AX.X,
                                    ALU.add).then_inc(qsum_done, 1)
            dve.wait_ge(qsum_done, 2)
            for s in range(CHUNKS):
                if s + 1 < CHUNKS:
                    layernorm(s + 1)
                else:
                    attention(0, 0, 2, 0, 16, 0, s)
                hidden_product(0, s, 0)
                if s == CHUNKS - 1:
                    attention(0, 0, 2, 0, 16, 1, s)
                hidden_product(0, s, 1)
                prepare(0, s)
                if s >= 1:
                    add_y(0, s - 1, 2, 0)
                for j in range(TPC):
                    if s + 1 < CHUNKS:
                        x_lo(TPC * (s + 1) + j)
                    qkv_bias(TPC * s + j)
                if s == CHUNKS - 1:
                    attention(0, 0, 2, 0, 16, 2, s + 1)
            with dve.Fori(0, LOOPS) as i:
                for s in range(CHUNKS, CHUNKS + STEPS):
                    for b in range(GB):
                        loop_attention(i, s, b)
                        hidden_product(i, s, b)
                    if past_last_block(s) and next_block(s) is not None:
                        with dve.If(i < LOOPS - 1):
                            prepare(i, s)
                    else:
                        prepare(i, s)
                    add_y(i, s - 1, 4, att_issued(s))
            add_y(LOOPS, CHUNKS - 1, 4, ATT_OPS)


def kernel(L0_attn_x, L0_attn_Wq, L0_attn_bq, L0_attn_Wk, L0_attn_bk, L0_attn_Wv, L0_attn_bv,
           L0_ffn_w1, L0_ffn_w1_scale, L0_ffn_w3, L0_ffn_w3_scale, L0_ffn_w2, L0_ffn_w2_scale):
    import numpy as np
    import concourse.bacc as bacc
    from concourse.bass_utils import run_bass_kernel_spmd

    def rows_first(w):
        n, k = w.shape
        return w.reshape(n // P, P, k // P, P).transpose(0, 3, 2, 1).reshape(n // P, P, k)

    w1, w3, w2 = (np.asarray(w) for w in (L0_ffn_w1, L0_ffn_w3, L0_ffn_w2))
    inter, dim = w1.shape
    w_all = np.stack([rows_first(w1), rows_first(w3), w2.T.reshape(inter // P, P, dim)], axis=2)
    scales = np.concatenate([np.asarray(L0_ffn_w1_scale), np.asarray(L0_ffn_w3_scale),
                             np.asarray(L0_ffn_w2_scale).T], axis=1)
    arrays = {
        "x": L0_attn_x, "wq": L0_attn_Wq, "bq": L0_attn_bq, "wk": L0_attn_Wk, "bk": L0_attn_bk,
        "wv": L0_attn_Wv, "bv": L0_attn_bv, "w_all": w_all, "scales": scales,
        "identity": np.eye(P, dtype=np.float32),
    }
    arrays = {name: np.ascontiguousarray(a) for name, a in arrays.items()}
    nc = bacc.Bacc("TRN2", target_bir_lowering=False, num_devices=1)
    args = [nc.dram_tensor(name, a.shape, mybir.dt.from_np(a.dtype), kind="ExternalInput").ap()
            for name, a in arrays.items()]
    out = nc.dram_tensor("out", arrays["x"].shape, F32, kind="ExternalOutput").ap()
    fused_block(nc, *args, out)
    result = run_bass_kernel_spmd(nc, [arrays], core_ids=[0])
    return result.results[0]["out"]
```

```python
from contextlib import ExitStack

import concourse.bass as bass
from concourse import mybir

F32 = mybir.dt.float32
F32R = mybir.dt.float32r
I32 = mybir.dt.int32
ALU = mybir.AluOpType
ACT = mybir.ActivationFunctionType
AX = mybir.AxisListType

P = 128
EPS = 1e-5
RSQRT_MAGIC = 0x5F3759DF
NEWTON = 3
WARM_UP = 14


def fused_block(nc: bass.Bass, x, wq, bq, wk, bk, wv, bv, w_all, scales, identity, out):
    B, S, E = x.shape
    T = B * S
    D, HKV = wk.shape[1], wk.shape[2]
    H = wq.shape[2]
    REP = H // HKV
    KB = E // P
    NBLK, _, MATS, _ = w_all.shape
    TILES = T // P
    CHUNK = 512
    TPC = CHUNK // P
    CHUNKS = T // CHUNK
    GB = 2
    GROUPS = NBLK // GB
    QKV = 3 * D * HKV
    DH = D * HKV
    RING = 2 * GB
    GATE, UP, DOWN = 0, 1, 2

    LOOPS = (GROUPS - 1) // 2
    STEPS = 2 * CHUNKS
    ATT = (TILES - 1) // LOOPS
    ATT_OPS = 10
    assert CHUNKS == TPC == KB == 4 and T == 2048 and E == 512 and D * REP * HKV == E and DH == P
    assert 1 + ATT * LOOPS == TILES and 1 + 2 * LOOPS == GROUPS and 3 * ATT <= 2 * STEPS

    x_tiles = x.rearrange("b s e -> (b s) e").rearrange("(t p) e -> t p e", p=P)
    out_tiles = out.rearrange("b s e -> (b s) e").rearrange("(t p) e -> t p e", p=P)
    qkv_spill = nc.dram_tensor("qkv_spill", [TILES, P, QKV], F32, kind="Internal").ap()

    with ExitStack() as ctx:
        def sb(name, shape, dt=F32):
            return ctx.enter_context(nc.sbuf_tensor(name, shape, dt))

        def sem(name):
            return ctx.enter_context(nc.semaphore(name))

        acc = sb("acc", [P, TILES, E])
        xT_hi = sb("xT_hi", [P, KB, T], F32R)
        xT_lo = sb("xT_lo", [P, KB, T], F32R)
        w_raw = sb("w_raw", [P, 2, MATS, E])
        w_hi = sb("w_hi", [P, RING, MATS, E], F32R)
        w_lo = sb("w_lo", [P, RING, MATS, E], F32R)
        h_hi = sb("h_hi", [P, 2, GB, CHUNK], F32R)
        h_lo = sb("h_lo", [P, 2, GB, CHUNK], F32R)
        hidden = sb("hidden", [P, GB, CHUNK])
        wqkv_hi = sb("wqkv_hi", [P, KB, QKV], F32R)
        wqkv_lo = sb("wqkv_lo", [P, KB, QKV], F32R)
        scratch = sb("scratch", [P, TPC, E])
        qkv = sb("qkv", [P, 3, QKV])
        bias = sb("bias", [P, QKV])
        scale = sb("scale", [P, NBLK, MATS * KB])
        ident = sb("ident", [P, P])
        scores = sb("scores", [P, D, D])
        top = sb("top", [P, D])
        total = sb("total", [P, D])
        att_out = sb("att_out", [P, DH])
        stats = sb("stats", [P, TPC, 6])
        mean_var = sb("mean_var", [P, TPC, 2])
        var = sb("var", [P, TPC])
        rstd = sb("rstd", [P, TPC])
        newton = sb("newton", [P, TPC])

        BORROWED = 8
        bq_raw = acc[:, 8, :]
        wq_sum = acc[:, 9, :].rearrange("p (kb n) -> p kb n", kb=KB)
        wk_raw = acc[:, 10, :].rearrange("p (kb n) -> p kb n", kb=KB)
        wv_raw = acc[:, 11, :].rearrange("p (kb n) -> p kb n", kb=KB)
        wq_raw = acc[:, 12:16, :]

        ps_gu = ctx.enter_context(nc.psum_tensor("ps_gu", [P, GB, 2, CHUNK], F32))
        ps_y = ctx.enter_context(nc.psum_tensor("ps_y", [P, 4, E], F32))

        def ps_t(t):
            return ps_y[:, t if t < TPC else (2, 0)[t % 2], :]

        def ps_qkv(t):
            return ps_y[:, (3, 1)[t % 2], 0:QKV]

        x_in = [sem(f"x_in{t}") for t in range(TILES)]
        ident_in, scale_in, bias_in, wqkv_in = sem("ident_in"), sem("scale_in"), sem("bias_in"), sem("wqkv_in")
        w_in = [sem(f"w_in{i}") for i in range(2)]
        qkv_out = [sem(f"qkv_out{i}") for i in range(2)]
        qkv_in = [sem(f"qkv_in{i}") for i in range(3)]
        stored = sem("stored")
        ln_ops, xn_done, t_done = sem("ln_ops"), sem("xn_done"), sem("t_done")
        xhi_done, xlo_done = sem("xhi_done"), sem("xlo_done")
        w_dequant, whi_done, wlo_done = sem("w_dequant"), sem("whi_done"), sem("wlo_done")
        w0_dequant = sem("w0_dequant")
        qsum_done, qkvw_hi, qkvw_lo = sem("qsum_done"), sem("qkvw_hi"), sem("qkvw_lo")
        qkv_done, qkv_evac = sem("qkv_done"), sem("qkv_evac")
        g_done, u_done, silu_done, prod_done = sem("g_done"), sem("u_done"), sem("silu_done"), sem("prod_done")
        hhi_done, hlo_done = sem("hhi_done"), sem("hlo_done")
        y_done, y_added = sem("y_done"), sem("y_added")
        att_ops, exp_done = sem("att_ops"), sem("exp_done")

        block = ctx.enter_context(nc.Block())

        def wait(eng, sem_, i, rate, n):
            if isinstance(i, int):
                if n + rate * i > 0:
                    eng.wait_ge(sem_, n + rate * i)
            else:
                eng.wait_ge(sem_, i * rate + n)

        def next_block(s):
            c = s % CHUNKS
            return GB * (s // CHUNKS + 1) + c - 1 if c in (1, 2) else None

        W_RATE = MATS * 2 * GB

        def block_index(i, n):
            if isinstance(i, int):
                return n
            return nc.s_assert_within(i * 2 * GB + n, n, NBLK - 1,
                                      skip_runtime_bounds_check_because="guarded by If in the last turn")

        def between_steps(s):
            n = next_block(s)
            order = []
            for j in range(TPC):
                tail = [("qkv", j)] if s + 1 == CHUNKS else [("qkv", j), ("transpose", j)]
                order += tail if j < TPC - 1 else tail[::-1]
                if n is not None and j in (0, 1, TPC - 1):
                    order.append(("weights", min(j, MATS - 1)))
            return order

        def dequant_operands(i, n, m):
            w = w_raw[:, n % 2, m].rearrange("p (j n) -> p j n", n=P)
            return w, scale[:, block_index(i, n), KB * m:KB * (m + 1)].unsqueeze(2).broadcast_to([P, KB, P])

        def att_piece(q):
            return divmod(q, 3) if q < 3 * ATT else None

        def past_last_block(s):
            return s >= 2 * CHUNKS

        @block.sync
        def _(sp):
            def load_w(i, n):
                if not isinstance(i, int) or n >= 2:
                    wait(sp, wlo_done, i, W_RATE, MATS * (n - 1))
                sp.dma_start(w_raw[:, n % 2], w_all[block_index(i, n)]).then_inc(w_in[n % 2], 16)

            def load_qkv(i, t, slot):
                sp.dma_start(qkv[:, slot], qkv_spill[i * ATT + t]).then_inc(qkv_in[slot], 16)

            for t in range(TPC):
                sp.dma_start(acc[:, t], x_tiles[t]).then_inc(x_in[t], 16)
            load_w(0, 0)
            load_w(0, 1)
            for t in range(TPC, BORROWED):
                sp.dma_start(acc[:, t], x_tiles[t]).then_inc(x_in[t], 16)
            sp.dma_start(wq_raw, wq.rearrange("(kb p) d h -> p kb (d h)", p=P)).then_inc(wqkv_in, 16)
            sp.dma_start(wk_raw, wk.rearrange("(kb p) d h -> p kb (d h)", p=P)).then_inc(wqkv_in, 16)
            sp.dma_start(wv_raw, wv.rearrange("(kb p) d h -> p kb (d h)", p=P)).then_inc(wqkv_in, 16)
            sp.dma_start(bq_raw, bq.rearrange("(o d) h -> o (d h)", o=1).broadcast_to([P, D * H])).then_inc(bias_in, 16)
            sp.dma_start(bias[:, DH:2 * DH], bk.rearrange("(o d) h -> o (d h)", o=1).broadcast_to([P, DH])).then_inc(bias_in, 16)
            sp.dma_start(bias[:, 2 * DH:], bv.rearrange("(o d) h -> o (d h)", o=1).broadcast_to([P, DH])).then_inc(bias_in, 16)
            sp.wait_ge(qkvw_lo, 3)
            sp.wait_ge(qsum_done, 2)
            for t in range(BORROWED, BORROWED + TPC):
                sp.dma_start(acc[:, t], x_tiles[t]).then_inc(x_in[t], 16)
            for c in range(CHUNKS):
                for t in range(TPC * c, TPC * c + TPC):
                    sp.wait_ge(qkv_evac, t + 1)
                    sp.dma_start(qkv_spill[t], qkv[:, t % 2]).then_inc(qkv_out[t % 2], 16)
                if c == 0:
                    for t in range(BORROWED + TPC, TILES):
                        sp.dma_start(acc[:, t], x_tiles[t]).then_inc(x_in[t], 16)
                    load_w(0, 2)
                    load_w(0, 3)
                if c == CHUNKS - 2:
                    sp.wait_ge(qkv_out[0], 16)
                    load_qkv(0, 0, 2)
            for slot in range(2):
                sp.wait_ge(qkv_out[slot], 16 * TILES // 2)
            with sp.Fori(0, LOOPS) as i:
                for s in range(CHUNKS, CHUNKS + STEPS):
                    for q in (2 * (s - CHUNKS), 2 * (s - CHUNKS) + 1):
                        piece = att_piece(q)
                        if piece and piece[1] == 0:
                            j = piece[0]
                            wait(sp, att_ops, i, ATT_OPS * ATT, ATT_OPS * (j if j == 0 else j - 1) + 7)
                            load_qkv(i, 1 + j, j % 2)
                    if s % CHUNKS == 0:
                        n = GB * (s // CHUNKS + 1)
                        if past_last_block(s):
                            with sp.If(i < LOOPS - 1):
                                load_w(i, n)
                                load_w(i, n + 1)
                        else:
                            load_w(i, n)
                            load_w(i, n + 1)
            for t in range(TILES):
                sp.wait_ge(y_added, TILES * (GROUPS - 1) + t + 1)
                sp.dma_start(out_tiles[t], acc[:, t]).then_inc(stored, 16)
            sp.wait_ge(stored, 16 * TILES)

        @block.tensor
        def _(pe):
            def transpose_tile(t):
                pe.wait_ge(xn_done, t + 1)
                if t >= TPC:
                    pe.wait_ge(xlo_done, t - 1)
                for kb in range(KB):
                    last = pe.transpose(ps_t(t)[:, kb * P:(kb + 1) * P], scratch[:, t % TPC, kb * P:(kb + 1) * P], ident[:])
                last.then_inc(t_done, 1)

            def qkv_tile(t):
                if t == 0:
                    pe.wait_ge(qkvw_lo, 3)
                if t >= 2:
                    pe.wait_ge(qkv_evac, t - 1)
                cols = slice(t * P, (t + 1) * P)
                parts = [(kb, xT_hi, w) for kb in range(KB) for w in (wqkv_hi, wqkv_lo)]
                parts += [(kb, xT_lo, wqkv_hi) for kb in range(KB)]
                for n, (kb, xt, w) in enumerate(parts):
                    last = pe.matmul(ps_qkv(t), xt[:, kb, cols], w[:, kb, :], start=(n == 0), stop=(n == 3 * KB - 1))
                last.then_inc(qkv_done, 1)

            def gate_up(i, s, b):
                c, g, k = s % CHUNKS, s // CHUNKS, GB * s + b
                n = GB * g + b
                cols = slice(c * CHUNK, (c + 1) * CHUNK)
                for m, done, freed in ((GATE, g_done, silu_done), (UP, u_done, prod_done)):
                    if c == 0:
                        wait(pe, whi_done, i, W_RATE, MATS * n + m + 1)
                    wait(pe, freed, i, GB * STEPS, k - 1)
                    hh, hl, lh = ([(kb, w, xt) for kb in range(KB)]
                                  for w, xt in ((w_hi, xT_hi), (w_hi, xT_lo), (w_lo, xT_hi)))
                    first = isinstance(i, int) and k == 0 and m == GATE
                    parts = (hh + hl if first else [part for pair in zip(hh, hl) for part in pair]) + lh
                    for n_part, (kb, w, xt) in enumerate(parts):
                        if isinstance(i, int) and b == 0 and m == GATE:
                            if n_part == 0:
                                pe.wait_ge(xhi_done, TPC * (c + 1))
                            if n_part == (KB if first else 1):
                                pe.wait_ge(xlo_done, TPC * (c + 1))
                        if c == 0 and n_part == 2 * KB:
                            wait(pe, wlo_done, i, W_RATE, MATS * n + m + 1)
                        last = pe.matmul(ps_gu[:, b, m, :], w[:, n % RING, m, kb * P:(kb + 1) * P], xt[:, kb, cols],
                                         start=(n_part == 0), stop=(n_part == 3 * KB - 1))
                    last.then_inc(done, 1)

            def down(i, s, banks):
                c, g = s % CHUNKS, s // CHUNKS
                if c == 0:
                    wait(pe, wlo_done, i, W_RATE, MATS * GB * (g + 1))
                wait(pe, hlo_done, i, GB * STEPS, GB * (s + 1))
                if banks == 4:
                    pe.wait_ge(qkv_evac, TILES)
                    wait(pe, y_added, i, TPC * STEPS, TPC * s)
                else:
                    pe.wait_ge(qkv_evac, TPC * (s + 1))
                for tt in range(TPC):
                    if banks == 2:
                        wait(pe, y_added, i, 0, TPC * s + tt - 1)
                    for b in range(GB):
                        last = down_part(s, tt, b, banks)
                    last.then_inc(y_done, 1)

            def down_part(s, tt, b, banks):
                r = (GB * (s // CHUNKS) + b) % RING
                rows = slice(tt * P, (tt + 1) * P)
                for n3, (h, w) in enumerate(((h_hi, w_hi), (h_hi, w_lo), (h_lo, w_hi))):
                    last = pe.matmul(ps_y[:, tt % banks, :], h[:, s % 2, b, rows], w[:, r, DOWN, :],
                                     start=(b == 0 and n3 == 0), stop=(b == GB - 1 and n3 == 2))
                return last

            def last_down(s):
                for b in range(GB):
                    pe.wait_ge(hlo_done, GB * s + b + 1)
                    for tt in range(TPC):
                        if b == 0:
                            pe.wait_ge(y_added, TPC * (s - 1) + tt + 1)
                        last = down_part(s, tt, b, TPC)
                        if b == GB - 1:
                            last.then_inc(y_done, 1)

            pe.wait_ge(ident_in, 16)
            pe.wait_ge(ln_ops, 2 * TPC)
            for n in range(WARM_UP):
                pe.transpose(ps_gu[:, 0, 0, 0:P], ident[:], ident[:])
            for t in range(TPC):
                transpose_tile(t)
            for s in range(CHUNKS):
                for b in range(GB):
                    gate_up(0, s, b)
                if s >= 1:
                    down(0, s - 1, 2)
                for what, j in between_steps(s):
                    if what == "qkv":
                        if s >= 1 and j == 1:
                            pe.wait_ge(y_added, TPC * s)
                        qkv_tile(TPC * s + j)
                    elif what == "transpose":
                        transpose_tile(TPC * (s + 1) + j)
            with pe.Fori(0, LOOPS) as i:
                for s in range(CHUNKS, CHUNKS + STEPS):
                    for b in range(GB):
                        gate_up(i, s, b)
                    down(i, s - 1, 4)
            last_down(CHUNKS * GROUPS - 1)

        @block.scalar
        def _(act):
            def split_hi(i, n, m):
                if isinstance(i, int) and n == 0:
                    act.wait_ge(w0_dequant, m + 1)
                else:
                    wait(act, w_dequant, i, W_RATE, MATS * (n - 1) + m + 1)
                if m == 0 and n >= RING:
                    wait(act, y_done, i, TPC * STEPS, TPC * CHUNKS * (n // GB - 1))
                nc.scalar.copy(w_hi[:, n % RING, m], w_raw[:, n % 2, m]).then_inc(whi_done, 1)

            def silu(i, s, b):
                k = GB * s + b
                wait(act, g_done, i, GB * STEPS, k + 1)
                wait(act, hlo_done, i, GB * STEPS, k - 1)
                nc.scalar.activation(hidden[:, b], ps_gu[:, b, GATE, :], ACT.Silu).then_inc(silu_done, 1)

            def hidden_hi(i, s, b):
                k = GB * s + b
                wait(act, prod_done, i, GB * STEPS, k + 1)
                wait(act, y_done, i, TPC * STEPS, TPC * (s - 1))
                nc.scalar.copy(h_hi[:, s % 2, b], hidden[:, b]).then_inc(hhi_done, 1)

            def x_hi(t):
                act.wait_ge(t_done, t + 1)
                nc.scalar.copy(xT_hi[:, :, t * P:(t + 1) * P],
                               ps_t(t).rearrange("p (kb n) -> p kb n", kb=KB)).then_inc(xhi_done, 1)

            def exponent(i, t):
                wait(act, att_ops, i, ATT_OPS * ATT, ATT_OPS * t + 4)
                nc.scalar.activation(scores[:], scores[:], ACT.Exp, scale=float(D) ** -0.5).then_inc(exp_done, 1)

            def prepare(i, s):
                n = next_block(s)
                if n is not None:
                    for m in range(MATS):
                        split_hi(i, n, m)

            act.dma_start(ident[:], identity).then_inc(ident_in, 16)
            act.dma_start(scale[:], scales.rearrange("(o n) m -> o n m", o=1)
                          .broadcast_to([P, NBLK, MATS * KB])).then_inc(scale_in, 16)
            split_hi(0, 0, 0)
            for t in range(TPC):
                x_hi(t)
            for n, m in ((0, 1), (0, 2), (1, 0), (1, 1), (1, 2)):
                split_hi(0, n, m)
            act.wait_ge(wqkv_in, 48)
            act.wait_ge(qsum_done, 1)
            for n, raw in enumerate((wq_sum, wk_raw, wv_raw)):
                nc.scalar.copy(wqkv_hi[:, :, n * DH:(n + 1) * DH], raw).then_inc(qkvw_hi, 1)
            for s in range(CHUNKS):
                for b in range(GB):
                    silu(0, s, b)
                    if s == CHUNKS - 1 and b == GB - 1:
                        exponent(0, 0)
                    hidden_hi(0, s, b)
                for what, j in between_steps(s):
                    if what == "transpose":
                        x_hi(TPC * (s + 1) + j)
                    elif what == "weights":
                        split_hi(0, next_block(s), j)
            with act.Fori(0, LOOPS) as i:
                for s in range(CHUNKS, CHUNKS + STEPS):
                    for b in range(GB):
                        silu(i, s, b)
                        piece = att_piece(2 * (s - CHUNKS) + b)
                        if piece and piece[1] == 0:
                            exponent(i, 1 + piece[0])
                        hidden_hi(i, s, b)
                    if past_last_block(s) and next_block(s) is not None:
                        with act.If(i < LOOPS - 1):
                            prepare(i, s)
                    else:
                        prepare(i, s)

        @block.gpsimd
        def _(pool):
            def split_lo(i, n, m):
                wait(pool, whi_done, i, W_RATE, MATS * n + m + 1)
                nc.gpsimd.tensor_tensor(w_lo[:, n % RING, m], w_raw[:, n % 2, m], w_hi[:, n % RING, m].bitcast(F32),
                                        ALU.subtract).then_inc(wlo_done, 1)

            def hidden_lo(i, s, b):
                wait(pool, hhi_done, i, GB * STEPS, GB * s + b + 1)
                nc.gpsimd.tensor_tensor(h_lo[:, s % 2, b], hidden[:, b], h_hi[:, s % 2, b].bitcast(F32),
                                        ALU.subtract).then_inc(hlo_done, 1)

            def prepare(i, s):
                n = next_block(s)
                if n is not None:
                    for m in range(MATS):
                        split_lo(i, n, m)

            pool.wait_ge(scale_in, 16)
            pool.wait_ge(w_in[0], 16)
            for m in range(MATS):
                w, w_scale = dequant_operands(0, 0, m)
                nc.gpsimd.tensor_tensor(w, w, w_scale, ALU.mult).then_inc(w0_dequant, 1)
            for n in range(2):
                for m in range(MATS):
                    split_lo(0, n, m)
            for n, raw in enumerate((wq_sum, wk_raw, wv_raw)):
                pool.wait_ge(qkvw_hi, n + 1)
                nc.gpsimd.tensor_tensor(wqkv_lo[:, :, n * DH:(n + 1) * DH], raw,
                                        wqkv_hi[:, :, n * DH:(n + 1) * DH].bitcast(F32),
                                        ALU.subtract).then_inc(qkvw_lo, 1)
            for s in range(CHUNKS):
                for b in range(GB):
                    hidden_lo(0, s, b)
                prepare(0, s)
            with pool.Fori(0, LOOPS) as i:
                for s in range(CHUNKS, CHUNKS + STEPS):
                    for b in range(GB):
                        hidden_lo(i, s, b)
                    if past_last_block(s) and next_block(s) is not None:
                        with pool.If(i < LOOPS - 1):
                            prepare(i, s)
                    else:
                        prepare(i, s)

        @block.vector
        def _(dve):
            ln = [0]

            def ln_op(ins):
                ln[0] += 1
                ins.then_inc(ln_ops, 1)

            def layernorm(c):
                for j in range(TPC):
                    dve.wait_ge(x_in[TPC * c + j], 16)
                    ln_op(nc.vector.bn_stats(stats[:, j], acc[:, TPC * c + j]))
                dve.wait_ge(ln_ops, ln[0])
                if c >= 1:
                    dve.wait_ge(xn_done, TPC * c)
                for j in range(TPC):
                    ln_op(nc.vector.bn_aggr(mean_var[:, j], stats[:, j]))
                dve.wait_ge(ln_ops, ln[0])
                ln_op(nc.vector.tensor_scalar(var[:], mean_var[:, :, 1], EPS, None, ALU.add))
                dve.wait_ge(ln_ops, ln[0])
                ln_op(nc.vector.tensor_scalar(newton[:].bitcast(I32), var[:].bitcast(I32), 1, None,
                                              ALU.logical_shift_right))
                dve.wait_ge(ln_ops, ln[0])
                ln_op(nc.vector.tensor_scalar(rstd[:].bitcast(I32), newton[:].bitcast(I32), -1.0,
                                              float(RSQRT_MAGIC), ALU.mult, ALU.add))
                for _ in range(NEWTON):
                    dve.wait_ge(ln_ops, ln[0])
                    ln_op(nc.vector.tensor_tensor(newton[:], rstd[:], rstd[:], ALU.mult))
                    dve.wait_ge(ln_ops, ln[0])
                    ln_op(nc.vector.scalar_tensor_tensor(out=newton[:], in0=newton[:], scalar=-0.5, in1=var[:],
                                                         op0=ALU.mult, op1=ALU.mult))
                    dve.wait_ge(ln_ops, ln[0])
                    ln_op(nc.vector.scalar_tensor_tensor(out=rstd[:], in0=newton[:], scalar=1.5, in1=rstd[:],
                                                         op0=ALU.add, op1=ALU.mult))
                dve.wait_ge(ln_ops, ln[0])
                if c >= 1:
                    dve.wait_ge(t_done, TPC * c)
                for j in range(TPC):
                    nc.vector.tensor_scalar(scratch[:, j], acc[:, TPC * c + j], mean_var[:, j, 0:1], rstd[:, j:j + 1],
                                            ALU.subtract, ALU.mult).then_inc(xn_done, 1)

            def x_lo(t):
                dve.wait_ge(xhi_done, t + 1)
                cols = slice(t * P, (t + 1) * P)
                nc.vector.tensor_tensor(xT_lo[:, :, cols], ps_t(t).rearrange("p (kb n) -> p kb n", kb=KB),
                                        xT_hi[:, :, cols].bitcast(F32), ALU.subtract).then_inc(xlo_done, 1)

            def dequant(i, n, m):
                if m == 0:
                    wait(dve, w_in[n % 2], i, 16 * GB, 16 * (n // 2 + 1))
                w, w_scale = dequant_operands(i, n, m)
                nc.vector.tensor_tensor(w, w, w_scale, ALU.mult).then_inc(w_dequant, 1)

            def prepare(i, s):
                n = next_block(s)
                if n is not None:
                    for m in range(MATS):
                        dequant(i, n, m)

            def qkv_bias(t):
                dve.wait_ge(qkv_done, t + 1)
                if t >= 2:
                    dve.wait_ge(qkv_out[t % 2], 16 * (t // 2))
                nc.vector.tensor_tensor(qkv[:, t % 2], ps_qkv(t), bias[:], ALU.add).then_inc(qkv_evac, 1)

            def hidden_product(i, s, b):
                k = GB * s + b
                wait(dve, silu_done, i, GB * STEPS, k + 1)
                wait(dve, u_done, i, GB * STEPS, k + 1)
                nc.vector.tensor_tensor(hidden[:, b], hidden[:, b], ps_gu[:, b, UP, :], ALU.mult).then_inc(prod_done, 1)

            def add_y(i, s, banks, att_count):
                c = s % CHUNKS
                wait(dve, y_added, i, TPC * STEPS, TPC * s)
                wait(dve, att_ops, i, ATT_OPS * ATT, att_count)
                for tt in range(TPC):
                    wait(dve, y_done, i, TPC * STEPS, TPC * s + tt + 1)
                    a = acc[:, TPC * c + tt]
                    nc.vector.tensor_tensor(a, a, ps_y[:, tt % banks, :], ALU.add).then_inc(y_added, 1)

            prod_deh = scratch[:].rearrange("p a b -> p (a b)").rearrange("p (d e h) -> p d e h", d=D, e=D)
            prod_dhe = scratch[:].rearrange("p a b -> p (a b)").rearrange("p (d h e) -> p d h e", d=D, h=HKV)

            def attention(i, t, slot, loads_rate, loads, piece, s):
                base = ATT_OPS * t

                def done(n):
                    wait(dve, att_ops, i, ATT_OPS * ATT, base + n)

                q = qkv[:, slot, 0:DH].rearrange("p (d h) -> p d h", d=D)
                k = qkv[:, slot, DH:2 * DH].rearrange("p (e h) -> p e h", e=D)
                v = qkv[:, slot, 2 * DH:].rearrange("p (e h) -> p h e", e=D)
                if piece == 0:
                    wait(dve, qkv_in[slot], i, loads_rate, loads)
                    done(0)
                    nc.vector.tensor_tensor(prod_deh, q.unsqueeze(2).broadcast_to([P, D, D, HKV]),
                                            k.unsqueeze(1).broadcast_to([P, D, D, HKV]), ALU.mult).then_inc(att_ops, 1)
                    done(1)
                    nc.vector.tensor_reduce(scores[:], prod_deh, AX.X, ALU.add).then_inc(att_ops, 1)
                    done(2)
                    nc.vector.tensor_reduce(top[:], scores[:], AX.X, ALU.max).then_inc(att_ops, 1)
                    done(3)
                    nc.vector.tensor_tensor(scores[:], scores[:], top[:].unsqueeze(2).broadcast_to([P, D, D]),
                                            ALU.subtract).then_inc(att_ops, 1)
                elif piece == 1:
                    wait(dve, exp_done, i, ATT, t + 1)
                    nc.vector.tensor_reduce(total[:], scores[:], AX.X, ALU.add).then_inc(att_ops, 1)
                    nc.vector.tensor_tensor(prod_dhe, scores[:].unsqueeze(2).broadcast_to([P, D, HKV, D]),
                                            v.unsqueeze(1).broadcast_to([P, D, HKV, D]), ALU.mult).then_inc(att_ops, 1)
                    done(5)
                    nc.vector.reciprocal(total[:], total[:]).then_inc(att_ops, 1)
                else:
                    done(6)
                    nc.vector.tensor_reduce(att_out[:].rearrange("p (d h) -> p d h", d=D), prod_dhe, AX.X,
                                            ALU.add).then_inc(att_ops, 1)
                    done(8)
                    o = att_out[:].rearrange("p (d h) -> p d h", d=D)
                    nc.vector.tensor_tensor(o, o, total[:].unsqueeze(2).broadcast_to([P, D, HKV]),
                                            ALU.mult).then_inc(att_ops, 1)
                    done(9)
                    wait(dve, y_added, i, TPC * STEPS, TPC * (s - 1))
                    a = acc[:, i * ATT + t].rearrange("p (n r) -> p n r", r=REP)
                    nc.vector.tensor_tensor(a, a, att_out[:].unsqueeze(2).broadcast_to([P, DH, REP]),
                                            ALU.add).then_inc(att_ops, 1)

            def loop_attention(i, s, slot_in_step):
                piece = att_piece(2 * (s - CHUNKS) + slot_in_step)
                if piece:
                    j = piece[0]
                    rate = (ATT + 1 - j % 2) // 2
                    attention(i, 1 + j, j % 2, 16 * rate, 16 * (j // 2 + 1), piece[1], s)

            def att_issued(s):
                per_piece = (4, 3, 3)
                slots = 2 * (s - CHUNKS + 1)
                return ATT_OPS + sum(per_piece[q % 3] for q in range(min(slots, 3 * ATT)))

            layernorm(0)
            for t in range(TPC):
                x_lo(t)
            dve.wait_ge(scale_in, 16)
            for m in range(MATS):
                dequant(0, 1, m)
            dve.wait_ge(wqkv_in, 48)
            nc.vector.tensor_reduce(wq_sum, wq_raw.rearrange("p kb (n r) -> p kb n r", r=REP), AX.X,
                                    ALU.add).then_inc(qsum_done, 1)
            for s in range(CHUNKS):
                if s + 1 < CHUNKS:
                    layernorm(s + 1)
                else:
                    attention(0, 0, 2, 0, 16, 0, s)
                hidden_product(0, s, 0)
                if s == 0:
                    dve.wait_ge(bias_in, 48)
                    nc.vector.tensor_reduce(bias[:, 0:DH], bq_raw.rearrange("p (n r) -> p n r", r=REP), AX.X,
                                            ALU.add).then_inc(qsum_done, 1)
                    dve.wait_ge(qsum_done, 2)
                hidden_product(0, s, 1)
                if s >= 1:
                    add_y(0, s - 1, 2, 0)
                if s == CHUNKS - 1:
                    attention(0, 0, 2, 0, 16, 1, s)
                for what, j in between_steps(s):
                    if what == "qkv":
                        qkv_bias(TPC * s + j)
                    elif what == "transpose":
                        x_lo(TPC * (s + 1) + j)
                    else:
                        dequant(0, next_block(s), j)
                if s == CHUNKS - 1:
                    attention(0, 0, 2, 0, 16, 2, s + 1)
            with dve.Fori(0, LOOPS) as i:
                for s in range(CHUNKS, CHUNKS + STEPS):
                    for b in range(GB):
                        loop_attention(i, s, b)
                        hidden_product(i, s, b)
                    if past_last_block(s) and next_block(s) is not None:
                        with dve.If(i < LOOPS - 1):
                            prepare(i, s)
                    else:
                        prepare(i, s)
                    add_y(i, s - 1, 4, att_issued(s))
            add_y(LOOPS, CHUNKS - 1, 4, ATT_OPS)


def kernel(L0_attn_x, L0_attn_Wq, L0_attn_bq, L0_attn_Wk, L0_attn_bk, L0_attn_Wv, L0_attn_bv,
           L0_ffn_w1, L0_ffn_w1_scale, L0_ffn_w3, L0_ffn_w3_scale, L0_ffn_w2, L0_ffn_w2_scale):
    import numpy as np
    import concourse.bacc as bacc
    from concourse.bass_utils import run_bass_kernel_spmd

    def rows_first(w):
        n, k = w.shape
        return w.reshape(n // P, P, k // P, P).transpose(0, 3, 2, 1).reshape(n // P, P, k)

    w1, w3, w2 = (np.asarray(w) for w in (L0_ffn_w1, L0_ffn_w3, L0_ffn_w2))
    inter, dim = w1.shape
    w_all = np.stack([rows_first(w1), rows_first(w3), w2.T.reshape(inter // P, P, dim)], axis=2)
    scales = np.concatenate([np.asarray(L0_ffn_w1_scale), np.asarray(L0_ffn_w3_scale),
                             np.asarray(L0_ffn_w2_scale).T], axis=1)
    arrays = {
        "x": L0_attn_x, "wq": L0_attn_Wq, "bq": L0_attn_bq, "wk": L0_attn_Wk, "bk": L0_attn_bk,
        "wv": L0_attn_Wv, "bv": L0_attn_bv, "w_all": w_all, "scales": scales,
        "identity": np.eye(P, dtype=np.float32),
    }
    arrays = {name: np.ascontiguousarray(a) for name, a in arrays.items()}
    nc = bacc.Bacc("TRN2", target_bir_lowering=False, num_devices=1)
    args = [nc.dram_tensor(name, a.shape, mybir.dt.from_np(a.dtype), kind="ExternalInput").ap()
            for name, a in arrays.items()]
    out = nc.dram_tensor("out", arrays["x"].shape, F32, kind="ExternalOutput").ap()
    fused_block(nc, *args, out)
    result = run_bass_kernel_spmd(nc, [arrays], core_ids=[0])
    return result.results[0]["out"]
```
